# Optimizing a Trainium2 kernel written in Bass

```python
import numpy as np
import jax
import jax.numpy as jnp

def _softmax(x, axis=-1):
    return jax.nn.softmax(x, axis=axis)

def _gelu(x):
    return jax.nn.gelu(x, approximate=True)

def _silu(x):
    return jax.nn.silu(x)

def _sigmoid(x):
    return jax.nn.sigmoid(x)

def _layernorm(x, axis=-1, eps=1e-05):
    m = jnp.mean(x, axis=axis, keepdims=True)
    v = jnp.var(x, axis=axis, keepdims=True)
    return (x - m) / jnp.sqrt(v + eps)

def _scatter_add(tgt, idx, src, axis=0):
    return tgt.at[idx].add(src)

def _segment_sum(src, seg, n):
    return jax.ops.segment_sum(src, seg, n)
kernel_name = 'mk_cond_resid_d1_seqx_r4_c7ddbc'

def setup_inputs(seed: int=0):
    np.random.seed(seed)
    _w = jnp.asarray

    def _rec_inputs():
        import jax
        import jax.numpy as jnp
        _rk = jax.random.key(seed)
        x = -0.000125 + 0.9999 * jax.random.normal(jax.random.fold_in(_rk, 1), (2, 1024, 256), jnp.float32)
        _lenS = 1024 - jax.random.randint(jax.random.fold_in(_rk, 7), (2,), 0, max(1, 1024 // 4) + 1, jnp.int32)
        _lenS2 = 1024 - jax.random.randint(jax.random.fold_in(_rk, 8), (2,), 0, max(1, 1024 // 4) + 1, jnp.int32)
        cond_1024 = -0.00493535 + 1.00056 * jax.random.normal(jax.random.fold_in(_rk, 11), (2, 256), jnp.float32)
        return (x, cond_1024)
    x, cond_1024 = _rec_inputs()

    def _L0_cond_setup():
        import jax, jax.numpy as jnp
        import numpy as np
        N, T, D, H = (64, 128, 256, 256)

        def lstm_scan(x, h0, Wx, Wh, b):
            xW = jnp.einsum('ntd,dg->ntg', x, Wx) + b
            Hdim = h0.shape[1]
            c0 = jnp.zeros_like(h0)

            def step(carry, xw_t):
                prev_h, prev_c = carry
                a = xw_t + prev_h @ Wh
                i = jax.nn.sigmoid(a[:, :Hdim])
                f = jax.nn.sigmoid(a[:, Hdim:2 * Hdim])
                o = jax.nn.sigmoid(a[:, 2 * Hdim:3 * Hdim])
                g = jnp.tanh(a[:, 3 * Hdim:])
                next_c = f * prev_c + i * g
                next_h = o * jnp.tanh(next_c)
                return ((next_h, next_c), next_h)
            _, hs = jax.lax.scan(step, (h0, c0), jnp.swapaxes(xW, 0, 1))
            return jnp.swapaxes(hs, 0, 1)
        key = jax.random.key(seed)
        k1, k2, k3, k4 = jax.random.split(key, 4)
        x = jax.random.normal(k1, (N, T, D), dtype=jnp.float32)
        h0 = jax.random.normal(k2, (N, H), dtype=jnp.float32)
        Wx = jax.random.normal(k3, (D, 4 * H), dtype=jnp.float32) / np.sqrt(D)
        Wh = jax.random.normal(k4, (H, 4 * H), dtype=jnp.float32) / np.sqrt(H)
        b = jnp.zeros((4 * H,), dtype=jnp.float32)
        return {'x': x, 'h0': h0, 'Wx': Wx, 'Wh': Wh, 'b': b}
    _L0_cond_all = _L0_cond_setup()
    _L0_cond_in = {k: v for k, v in _L0_cond_all.items() if k in ('Wx', 'Wh', 'b')}
    del _L0_cond_all
    return {'x': x, 'cond_1024': cond_1024, 'L0_cond_Wx': _L0_cond_in['Wx'], 'L0_cond_Wh': _L0_cond_in['Wh'], 'L0_cond_b': _L0_cond_in['b']}

def reference(x, cond_1024, L0_cond_Wx, L0_cond_Wh, L0_cond_b):
    import jax
    import jax.numpy as jnp

    def _L0_cond_ref(x, h0, Wx, Wh, b):
        import jax, jax.numpy as jnp
        import numpy as np
        N, T, D, H = (64, 128, 256, 256)

        def lstm_scan(x, h0, Wx, Wh, b):
            xW = jnp.einsum('ntd,dg->ntg', x, Wx) + b
            Hdim = h0.shape[1]
            c0 = jnp.zeros_like(h0)

            def step(carry, xw_t):
                prev_h, prev_c = carry
                a = xw_t + prev_h @ Wh
                i = jax.nn.sigmoid(a[:, :Hdim])
                f = jax.nn.sigmoid(a[:, Hdim:2 * Hdim])
                o = jax.nn.sigmoid(a[:, 2 * Hdim:3 * Hdim])
                g = jnp.tanh(a[:, 3 * Hdim:])
                next_c = f * prev_c + i * g
                next_h = o * jnp.tanh(next_c)
                return ((next_h, next_c), next_h)
            _, hs = jax.lax.scan(step, (h0, c0), jnp.swapaxes(xW, 0, 1))
            return jnp.swapaxes(hs, 0, 1)
        return lstm_scan(x, h0, Wx, Wh, b)
    x = x + _L0_cond_ref(x, cond_1024, L0_cond_Wx, L0_cond_Wh, L0_cond_b)
    return x

_drawn_inputs = setup_inputs


def setup_inputs(seed=0):
    import zlib

    import numpy as np

    out = dict(_drawn_inputs(seed))
    spreads = {'L0_cond_b': (0.0, 0.1)}
    factors = {}
    for name, (base, spread) in spreads.items():
        noise = np.random.default_rng([zlib.crc32(name.encode()), seed]).standard_normal(out[name].shape)
        drawn = base * np.exp(spread * noise) if base else spread * noise
        out[name] = jnp.asarray(drawn.astype(out[name].dtype))
    for name, factor in factors.items():
        out[name] = (out[name] * factor).astype(out[name].dtype)
    return out
```

```python
from contextlib import ExitStack

import concourse.bass as bass
from concourse import mybir

F32 = mybir.dt.float32
ALU = mybir.AluOpType
ACT = mybir.ActivationFunctionType

P = 128
U = 8
GATES = [2, 0, 1, 3]
O, I, F, G = range(4)


def lstm_residual(nc, x_t, h0_t, w_x, w_h, bias, out_t):
    D, T, B = x_t.shape
    H = h0_t.shape[0]
    KD, M = D // P, H // P
    S = M * B
    A = 4 * S
    TB = 512 // B
    NB = T // TB

    with ExitStack() as ctx:
        def sb(name, shape):
            return ctx.enter_context(nc.sbuf_tensor(name, shape, F32))

        def sem(name):
            return ctx.enter_context(nc.semaphore(name))

        x_sb = sb("x_sb", [P, KD, T, B])
        wx_sb = sb("wx_sb", [P, KD, 4 * H])
        wh_sb = sb("wh_sb", [P, M, 4 * H])
        bias_sb = sb("bias_sb", [P, 4 * M])
        xw_sb = sb("xw_sb", [P, T, 4, M, B])
        ident = sb("ident", [P, P])
        h_ring = sb("h_ring", [P, U, M, B])
        acts = sb("acts", [P, 2, 5, S])
        prods = sb("prods", [P, 2, 2, S])
        tanh_c = sb("tanh_c", [P, 2, S])
        out_sb = sb("out_sb", [P, M, T, B])
        gate_ps = [ctx.enter_context(nc.psum_tensor(f"gate_ps{i}", [P, 512], F32)) for i in range(2)]
        xw_ps = [ctx.enter_context(nc.psum_tensor(f"xw_ps{i}", [P, 512], F32)) for i in range(4)]

        x_in = sem("x_in")
        wx_in = sem("wx_in")
        wh_in = sem("wh_in")
        h0_in = sem("h0_in")
        ident_made = sem("ident_made")
        wh_scaled = sem("wh_scaled")
        h0_doubled = sem("h0_doubled")
        c0_cleared = sem("c0_cleared")
        xw_done = sem("xw_done")
        xw_copied = sem("xw_copied")
        gates_done = sem("gates_done")
        acts_done = sem("acts_done")
        prods_done = sem("prods_done")
        c_done = sem("c_done")
        tanh_c_done = sem("tanh_c_done")
        h_done = sem("h_done")
        out_done = sem("out_done")
        out_stored = sem("out_stored")

        block = ctx.enter_context(nc.Block())

        @block.sync
        def _(sp):
            sp.dma_start(wx_sb[:], w_x.rearrange("(k p) n -> p k n", p=P)).then_inc(wx_in, 16)
            sp.dma_start(bias_sb[:], bias).then_inc(wx_in, 16)
            sp.dma_start(x_sb[:], x_t.rearrange("(k p) t b -> p k t b", p=P)).then_inc(x_in, 16)
            sp.dma_start(wh_sb[:], w_h.rearrange("(k p) n -> p k n", p=P)).then_inc(wh_in, 16)
            sp.dma_start(h_ring[:, U - 1], h0_t.rearrange("(m p) b -> p m b", p=P)).then_inc(h0_in, 16)
            out_v = out_t.rearrange("(m p) t b -> p m t b", p=P)
            for n in range(4):
                sp.wait_ge(out_done, T // U // 4 * (n + 1))
                ts = slice(T // 4 * n, T // 4 * (n + 1))
                sp.dma_start(out_v[:, :, ts], out_sb[:, :, ts]).then_inc(out_stored, 16)
            sp.wait_ge(out_stored, 64)

        @block.gpsimd
        def _(pool):
            pool.memset(ident[:], 0.0).then_inc(ident_made, 1)
            pool.wait_ge(ident_made, 1)
            pool.affine_select(out=ident[:], in_=ident[:], compare_op=ALU.not_equal, fill=1.0, base=0,
                               pattern=[[-1, P]], channel_multiplier=1).then_inc(ident_made, 1)

        @block.tensor
        def _(pe):
            pe.wait_ge(wx_in, 32)
            pe.wait_ge(x_in, 16)
            for n in range(NB):
                for c in range(4 * M):
                    q = n * 4 * M + c
                    if q >= 4:
                        pe.wait_ge(xw_copied, q - 3)
                    g, m = GATES[c // M], c % M
                    for k in range(KD):
                        mm = pe.matmul(xw_ps[q % 4][:, :], wx_sb[:, k, g * H + m * P:g * H + (m + 1) * P],
                                       x_sb[:, k, n * TB:(n + 1) * TB, :],
                                       start=(k == 0), stop=(k == KD - 1))
                    mm.then_inc(xw_done, 1)
            pe.wait_ge(ident_made, 2)
            pe.wait_ge(wh_scaled, 2)
            pe.wait_ge(xw_copied, NB * 4 * M)
            pe.wait_ge(h0_doubled, 1)
            with pe.Fori(0, T // U) as r:
                for u in range(U):
                    ps = gate_ps[u % 2]
                    pe.matmul(ps[:, 0:A], ident[:], xw_sb[:, bass.ds(r * U + u, 1)], start=True, stop=False,
                              skip_group_check=True)
                    pe.wait_ge(h_done, r * U + u)
                    for c in range(4 * M):
                        g, m = GATES[c // M], c % M
                        for k in range(M):
                            mm = pe.matmul(ps[:, B * c:B * c + B],
                                           wh_sb[:, k, g * H + m * P:g * H + (m + 1) * P],
                                           h_ring[:, (u - 1) % U, k, :], start=False,
                                           stop=(c == 4 * M - 1 and k == M - 1), skip_group_check=True)
                    mm.then_inc(gates_done, 1)

        @block.scalar
        def _(act):
            with act.Fori(0, T // U) as r:
                for u in range(U):
                    p = u % 2
                    act.wait_ge(gates_done, r * U + u + 1)
                    act.activation(acts[:, p, 0:4, :], gate_ps[p][:, 0:A], ACT.Tanh).then_inc(acts_done, 1)
                    act.wait_ge(c_done, r * U + u + 1)
                    act.activation(tanh_c[:, p, :], acts[:, 1 - p, 4, :], ACT.Tanh, scale=0.5)\
                        .then_inc(tanh_c_done, 1)

        @block.vector
        def _(dve):
            dve.memset(acts[:, 0, 4, :], 0.0).then_inc(c0_cleared, 1)
            for n in range(NB):
                for c in range(4 * M):
                    q = n * 4 * M + c
                    g, m = c // M, c % M
                    dve.wait_ge(xw_done, q + 1)
                    j = GATES[g] * M + m
                    dve.tensor_scalar(xw_sb[:, n * TB:(n + 1) * TB, g, m, :], xw_ps[q % 4][:, :]
                                      .rearrange("p (t b) -> p t b", b=B), bias_sb[:, j:j + 1],
                                      1.0 if g == G else 0.5, ALU.add, ALU.mult).then_inc(xw_copied, 1)
            dve.wait_ge(wh_in, 16)
            dve.tensor_scalar(wh_sb[:, :, 0:3 * H], wh_sb[:, :, 0:3 * H], 0.25, None, ALU.mult)\
               .then_inc(wh_scaled, 1)
            dve.tensor_scalar(wh_sb[:, :, 3 * H:], wh_sb[:, :, 3 * H:], 0.5, None, ALU.mult)\
               .then_inc(wh_scaled, 1)
            dve.wait_ge(h0_in, 16)
            dve.tensor_scalar(h_ring[:, U - 1], h_ring[:, U - 1], 2.0, None, ALU.mult).then_inc(h0_doubled, 1)
            dve.wait_ge(c0_cleared, 1)
            with dve.Fori(0, T // U) as r:
                for u in range(U):
                    p = u % 2
                    dve.wait_ge(acts_done, r * U + u + 1)
                    dve.scalar_tensor_tensor(out=prods[:, p], in0=acts[:, p, I:F + 1], scalar=1.0,
                                             in1=acts[:, p, G:G + 2], op0=ALU.add, op1=ALU.mult)\
                       .then_inc(prods_done, 1)
                    dve.wait_ge(prods_done, r * U + u + 1)
                    dve.scalar_tensor_tensor(out=acts[:, 1 - p, 4], in0=prods[:, p, 1], scalar=0.5,
                                             in1=prods[:, p, 0], op0=ALU.mult, op1=ALU.add)\
                       .then_inc(c_done, 1)
                    dve.wait_ge(tanh_c_done, r * U + u + 1)
                    dve.scalar_tensor_tensor(out=h_ring[:, u].rearrange("p m b -> p (m b)"),
                                             in0=acts[:, p, O], scalar=1.0, in1=tanh_c[:, p],
                                             op0=ALU.add, op1=ALU.mult).then_inc(h_done, 1)
                dve.wait_ge(h_done, r * U + U)
                for m in range(M):
                    ins = dve.scalar_tensor_tensor(out=out_sb[:, m, bass.ds(r * U, U)], in0=h_ring[:, :, m, :],
                                                   scalar=0.5, in1=x_sb[:, m, bass.ds(r * U, U)],
                                                   op0=ALU.mult, op1=ALU.add)
                ins.then_inc(out_done, 1)


def kernel(**inputs):
    import numpy as np
    import concourse.bacc as bacc
    from concourse.bass_utils import run_bass_kernel_spmd

    x = np.asarray(inputs["x"])
    arrays = {
        "x_t": np.ascontiguousarray(x.transpose(2, 1, 0)),
        "h0_t": np.ascontiguousarray(np.asarray(inputs["cond_1024"]).T),
        "w_x": np.ascontiguousarray(inputs["L0_cond_Wx"]),
        "w_h": np.ascontiguousarray(inputs["L0_cond_Wh"]),
        "bias": np.ascontiguousarray(np.asarray(inputs["L0_cond_b"]).reshape(-1, P).T),
    }
    nc = bacc.Bacc("TRN2", target_bir_lowering=False, num_devices=1)
    args = [nc.dram_tensor(n, a.shape, F32, kind="ExternalInput").ap() for n, a in arrays.items()]
    out = nc.dram_tensor("out_t", arrays["x_t"].shape, F32, kind="ExternalOutput").ap()
    lstm_residual(nc, *args, out)
    r = run_bass_kernel_spmd(nc, [arrays], core_ids=[0])
    return np.ascontiguousarray(r.results[0]["out_t"].transpose(2, 1, 0))
```

```python
from contextlib import ExitStack

import concourse.bass as bass
from concourse import mybir

F32 = mybir.dt.float32
F16 = mybir.dt.float16
I32 = mybir.dt.int32
ALU = mybir.AluOpType
ACT = mybir.ActivationFunctionType
AX = mybir.AxisListType
RMAX = bass.bass_isa.ReduceOp.max

P = 128
U = 8
GATES = [2, 0, 1, 3]
O, I, F, G = range(4)
H_BITS = 14
W_TOP = 14
LEAST = 2.0 ** -46


def lstm_residual(nc, x_t, h0_t, w_x, w_h, bias, out_t):
    D, T, B = x_t.shape
    H = h0_t.shape[0]
    KD, M = D // P, H // P
    S = M * B
    C = 4 * M
    TB = 512 // B
    NB = T // TB

    with ExitStack() as ctx:
        def sb(name, shape, dt=F32):
            return ctx.enter_context(nc.sbuf_tensor(name, shape, dt))

        def sem(name):
            return ctx.enter_context(nc.semaphore(name))

        x_sb = sb("x_sb", [P, KD, T, B])
        wx_sb = sb("wx_sb", [P, KD, 4 * H])
        wh_sb = sb("wh_sb", [P, M, 4 * H])
        w_hi = sb("w_hi", [P, M, 4 * H], F16)
        w_lo = sb("w_lo", [P, M, 4 * H], F16)
        w_scaled = sb("w_scaled", [P, M, 4 * H])
        bias_sb = sb("bias_sb", [P, C])
        w_max = sb("w_max", [P, 1])
        w_top = sb("w_top", [P, 1])
        scale_w = sb("scale_w", [P, 1])
        scale_a = sb("scale_a", [P, 2])
        unscale = sb("unscale", [P, 1])
        xw_sb = sb("xw_sb", [P, T, C, B])
        ident = sb("ident", [P, P])
        h0_sb = sb("h0_sb", [P, M, B])
        h_parts = sb("h_parts", [P, 2, M, 2, B], F16)
        h_ring = sb("h_ring", [P, U, M, B])
        sums = sb("sums", [P, 2, C * B])
        acts = sb("acts", [P, 2, 5, S])
        o_gate = sb("o_gate", [P, 2, S])
        prods = sb("prods", [P, 2, 2, S])
        tanh_c = sb("tanh_c", [P, 2, S])
        out_sb = sb("out_sb", [P, M, T, B])
        gate_ps = [ctx.enter_context(nc.psum_tensor(f"gate_ps{i}", [P, 512], F32)) for i in range(2)]
        xw_ps = [ctx.enter_context(nc.psum_tensor(f"xw_ps{i}", [P, 512], F32)) for i in range(4)]

        x_in = sem("x_in")
        wx_in = sem("wx_in")
        wh_in = sem("wh_in")
        h0_in = sem("h0_in")
        ident_made = sem("ident_made")
        w_max_done = sem("w_max_done")
        w_top_done = sem("w_top_done")
        scales_done = sem("scales_done")
        w_cut = sem("w_cut")
        h0_scaled = sem("h0_scaled")
        xw_done = sem("xw_done")
        xw_copied = sem("xw_copied")
        ps_cleared = sem("ps_cleared")
        gates_done = sem("gates_done")
        sums_done = sem("sums_done")
        acts_done = sem("acts_done")
        prods_done = sem("prods_done")
        c_done = sem("c_done")
        o_done = sem("o_done")
        tanh_c_done = sem("tanh_c_done")
        h_hi_done = sem("h_hi_done")
        h_done = sem("h_done")
        h_lo_done = sem("h_lo_done")
        out_done = sem("out_done")
        out_stored = sem("out_stored")

        block = ctx.enter_context(nc.Block())

        @block.sync
        def _(sp):
            sp.dma_start(wh_sb[:], w_h.rearrange("(k p) n -> p k n", p=P)).then_inc(wh_in, 16)
            sp.dma_start(wx_sb[:], w_x.rearrange("(k p) n -> p k n", p=P)).then_inc(wx_in, 16)
            sp.dma_start(bias_sb[:], bias).then_inc(wx_in, 16)
            sp.dma_start(x_sb[:], x_t.rearrange("(k p) t b -> p k t b", p=P)).then_inc(x_in, 16)
            sp.dma_start(h0_sb[:], h0_t.rearrange("(m p) b -> p m b", p=P)).then_inc(h0_in, 16)
            out_v = out_t.rearrange("(m p) t b -> p m t b", p=P)
            for n in range(4):
                sp.wait_ge(out_done, T // U // 4 * (n + 1))
                ts = slice(T // 4 * n, T // 4 * (n + 1))
                sp.dma_start(out_v[:, :, ts], out_sb[:, :, ts]).then_inc(out_stored, 16)
            sp.wait_ge(out_stored, 64)

        @block.gpsimd
        def _(pool):
            pool.memset(ident[:], 0.0).then_inc(ident_made, 1)
            pool.wait_ge(ident_made, 1)
            pool.affine_select(out=ident[:], in_=ident[:], compare_op=ALU.not_equal, fill=1.0, base=0,
                               pattern=[[-1, P]], channel_multiplier=1).then_inc(ident_made, 1)
            pool.wait_ge(w_max_done, 1)
            pool.partition_all_reduce(w_top[:], w_max[:], P, RMAX).then_inc(w_top_done, 1)

        def w_tile(w, c, k):
            at = GATES[c // M] * H + c % M * P
            return w[:, k, at:at + P]

        @block.tensor
        def _(pe):
            pe.wait_ge(wx_in, 32)
            pe.wait_ge(x_in, 16)
            for n in range(NB):
                for c in range(C):
                    q = n * C + c
                    if q >= 4:
                        pe.wait_ge(xw_copied, q - 3)
                    for k in range(KD):
                        mm = pe.matmul(xw_ps[q % 4][:, :], w_tile(wx_sb, c, k),
                                       x_sb[:, k, n * TB:(n + 1) * TB, :],
                                       start=(k == 0), stop=(k == KD - 1))
                    mm.then_inc(xw_done, 1)

            def step_ps(p):
                return gate_ps[p][:, 0:C * 2 * B].rearrange("p (c s b) -> p c s b", c=C, s=2)

            def put_inputs(p, t):
                pe.matmul(step_ps(p)[:, :, 0, :], ident[:], xw_sb[:, t], start=True, stop=False,
                          skip_group_check=True)

            def product(p):
                h = h_parts[:, 1 - p]
                for c in range(C):
                    for k in range(M):
                        pe.matmul(step_ps(p)[:, c, 0, :], w_tile(w_lo, c, k), h[:, k, 0, :],
                                  start=False, stop=False, skip_group_check=True)
                yield
                for c in range(C):
                    for k in range(M):
                        mm = pe.matmul(step_ps(p)[:, c], w_tile(w_hi, c, k), h[:, k],
                                       start=False, stop=(c == C - 1 and k == M - 1), skip_group_check=True)
                mm.then_inc(gates_done, 1)

            def steps(r, n):
                for u in range(n):
                    p = (u + 1) % 2
                    put_inputs(p, bass.ds(r * U + u + 1, 1))
                    halves = product(p)
                    pe.wait_ge(h_hi_done, r * U + u + 1)
                    next(halves)
                    pe.wait_ge(h_lo_done, r * U + u + 1)
                    next(halves, None)

            pe.wait_ge(ident_made, 2)
            pe.wait_ge(xw_copied, NB * C)
            pe.wait_ge(h0_scaled, 1)
            pe.wait_ge(ps_cleared, 1)
            put_inputs(0, slice(0, 1))
            for c in range(C):
                for k in range(M):
                    mm = pe.matmul(step_ps(0)[:, c, 0, :], w_tile(wh_sb, c, k), h0_sb[:, k, :],
                                   start=False, stop=True, skip_group_check=True)
            mm.then_inc(gates_done, 1)
            pe.wait_ge(w_cut, 4)
            with pe.Fori(0, T // U - 1) as r:
                steps(r, U)
            steps(T // U - 1, U - 1)

        @block.scalar
        def _(act):
            act.wait_ge(scales_done, 4)
            with act.Fori(0, T // U) as r:
                for u in range(U):
                    p = u % 2
                    act.wait_ge(sums_done, r * U + u + 1)
                    act.activation(acts[:, p, 0:4, :], sums[:, p], ACT.Tanh, scale=unscale[:, 0:1])\
                        .then_inc(acts_done, 1)
                    act.wait_ge(c_done, r * U + u + 1)
                    act.activation(tanh_c[:, p, :], acts[:, 1 - p, 4, :], ACT.Tanh, scale=0.5)\
                        .then_inc(tanh_c_done, 1)

        @block.vector
        def _(dve):
            dve.wait_ge(wh_in, 16)
            dve.tensor_reduce(w_max[:], wh_sb[:], AX.XY, ALU.max, apply_absolute_value=True)\
               .then_inc(w_max_done, 1)
            dve.memset(acts[:, 0, 4, :], 0.0)
            dve.memset(gate_ps[0][:, 0:C * 2 * B], 0.0).then_inc(ps_cleared, 1)
            dve.wait_ge(w_top_done, 1)
            top_bits = w_top[:].bitcast(I32)
            dve.tensor_scalar(top_bits, top_bits, 0x7F800000, None, ALU.bitwise_and).then_inc(w_top_done, 1)
            dve.wait_ge(w_top_done, 2)
            dve.tensor_scalar(w_top[:], w_top[:], LEAST, None, ALU.max).then_inc(w_top_done, 1)
            dve.wait_ge(w_top_done, 3)
            dve.tensor_scalar(scale_w[:].bitcast(I32), top_bits, -1.0, float((254 + W_TOP) << 23),
                              ALU.mult, ALU.add).then_inc(scales_done, 1)
            dve.tensor_scalar(unscale[:], w_top[:], 2.0 ** -(W_TOP + H_BITS), None, ALU.mult)\
               .then_inc(scales_done, 1)
            dve.wait_ge(scales_done, 2)
            dve.tensor_scalar(scale_a[:, 0:1], scale_w[:], 2.0 ** (H_BITS - 1), None, ALU.mult)\
               .then_inc(scales_done, 1)
            dve.tensor_scalar(scale_a[:, 1:2], scale_w[:], 2.0 ** H_BITS, None, ALU.mult)\
               .then_inc(scales_done, 1)
            dve.wait_ge(scales_done, 4)
            for n in range(NB):
                for c in range(C):
                    q = n * C + c
                    dve.wait_ge(xw_done, q + 1)
                    j = GATES[c // M] * M + c % M
                    g = int(c // M == G)
                    dve.tensor_scalar(xw_sb[:, n * TB:(n + 1) * TB, c, :],
                                      xw_ps[q % 4][:, :].rearrange("p (t b) -> p t b", b=B),
                                      bias_sb[:, j:j + 1], scale_a[:, g:g + 1], ALU.add, ALU.mult)\
                       .then_inc(xw_copied, 1)
            dve.tensor_scalar(wh_sb[:, :, 0:3 * H], wh_sb[:, :, 0:3 * H], 0.5, None, ALU.mult)\
               .then_inc(w_cut, 1)
            dve.wait_ge(h0_in, 16)
            dve.tensor_scalar(h0_sb[:], h0_sb[:], scale_a[:, 1:2], None, ALU.mult)\
               .then_inc(h0_scaled, 1)
            dve.wait_ge(w_cut, 1)
            dve.tensor_scalar(w_scaled[:], wh_sb[:], scale_w[:, 0:1], None, ALU.mult).then_inc(w_cut, 1)
            dve.tensor_scalar(w_hi[:], wh_sb[:], scale_w[:, 0:1], None, ALU.mult).then_inc(w_cut, 1)
            dve.wait_ge(w_cut, 3)
            dve.tensor_tensor(w_lo[:], w_scaled[:], w_hi[:], ALU.subtract).then_inc(w_cut, 1)

            with dve.Fori(0, T // U) as r:
                for u in range(U):
                    p = u % 2
                    dve.wait_ge(gates_done, r * U + u + 1)
                    dve.tensor_reduce(sums[:, p].rearrange("p (c b) -> p c b", b=B),
                                      gate_ps[p][:, 0:C * 2 * B]
                                      .rearrange("p (c s b) -> p c b s", c=C, s=2), AX.X, ALU.add)\
                       .then_inc(sums_done, 1)
                    dve.wait_ge(acts_done, r * U + u + 1)
                    dve.scalar_tensor_tensor(out=prods[:, p], in0=acts[:, p, I:F + 1], scalar=1.0,
                                             in1=acts[:, p, G:G + 2], op0=ALU.add, op1=ALU.mult)\
                       .then_inc(prods_done, 1)
                    dve.wait_ge(prods_done, r * U + u + 1)
                    dve.scalar_tensor_tensor(out=acts[:, 1 - p, 4], in0=prods[:, p, 1], scalar=0.5,
                                             in1=prods[:, p, 0], op0=ALU.mult, op1=ALU.add)\
                       .then_inc(c_done, 1)
                    dve.tensor_scalar(o_gate[:, p], acts[:, p, O], 1.0, 2.0 ** (H_BITS - 1),
                                      ALU.add, ALU.mult).then_inc(o_done, 1)
                    dve.wait_ge(o_done, r * U + u + 1)
                    dve.wait_ge(tanh_c_done, r * U + u + 1)
                    o, tc = (a[:, p].rearrange("p (m b) -> p m b", b=B) for a in (o_gate, tanh_c))
                    dve.tensor_tensor(h_parts[:, p, :, 0, :], o, tc, ALU.mult).then_inc(h_hi_done, 1)
                    dve.tensor_tensor(h_ring[:, u], o, tc, ALU.mult).then_inc(h_done, 1)
                    dve.wait_ge(h_done, r * U + u + 1)
                    dve.wait_ge(h_hi_done, r * U + u + 1)
                    dve.tensor_tensor(h_parts[:, p, :, 1, :], h_ring[:, u], h_parts[:, p, :, 0, :],
                                      ALU.subtract).then_inc(h_lo_done, 1)
                for m in range(M):
                    ins = dve.scalar_tensor_tensor(out=out_sb[:, m, bass.ds(r * U, U)], in0=h_ring[:, :, m, :],
                                                   scalar=2.0 ** -H_BITS, in1=x_sb[:, m, bass.ds(r * U, U)],
                                                   op0=ALU.mult, op1=ALU.add)
                ins.then_inc(out_done, 1)


def kernel(**inputs):
    import numpy as np
    import concourse.bacc as bacc
    from concourse.bass_utils import run_bass_kernel_spmd

    x = np.asarray(inputs["x"])
    arrays = {
        "x_t": np.ascontiguousarray(x.transpose(2, 1, 0)),
        "h0_t": np.ascontiguousarray(np.asarray(inputs["cond_1024"]).T),
        "w_x": np.ascontiguousarray(inputs["L0_cond_Wx"]),
        "w_h": np.ascontiguousarray(inputs["L0_cond_Wh"]),
        "bias": np.ascontiguousarray(np.asarray(inputs["L0_cond_b"]).reshape(-1, P).T),
    }
    nc = bacc.Bacc("TRN2", target_bir_lowering=False, num_devices=1)
    args = [nc.dram_tensor(n, a.shape, F32, kind="ExternalInput").ap() for n, a in arrays.items()]
    out = nc.dram_tensor("out_t", arrays["x_t"].shape, F32, kind="ExternalOutput").ap()
    lstm_residual(nc, *args, out)
    r = run_bass_kernel_spmd(nc, [arrays], core_ids=[0])
    return np.ascontiguousarray(r.results[0]["out_t"].transpose(2, 1, 0))
```

```python
from contextlib import ExitStack

import concourse.bass as bass
from concourse import mybir

F32 = mybir.dt.float32
F16 = mybir.dt.float16
BF16 = mybir.dt.bfloat16
I32 = mybir.dt.int32
ALU = mybir.AluOpType
ACT = mybir.ActivationFunctionType
AX = mybir.AxisListType
RMAX = bass.bass_isa.ReduceOp.max

P = 128
U = 16
AHEAD = 2
LAG = 2
GATES = [2, 0, 1, 3]
O, I, F, G = range(4)
H_BITS = 14
W_TOP = 14
X_PARTS = 3
LEAST = 2.0 ** -46


def lstm_residual(nc, x_p, h0_p, w_x, w_h, bias, out_p):
    _, T, KD, B = x_p.shape
    M = h0_p.shape[1]
    H = M * P
    C = M * 4
    R = T // U
    UB = U * B
    STORES = [R // 2, R // 4 * 3, R - 2, R + 1]

    with ExitStack() as ctx:
        def sb(name, shape, dt=F32):
            return ctx.enter_context(nc.sbuf_tensor(name, shape, dt))

        def bank(name):
            return ctx.enter_context(nc.psum_tensor(name, [P, 512], F32))

        def sem(name):
            return ctx.enter_context(nc.semaphore(name))

        def sems(name):
            return [sem(f"{name}{m}") for m in range(M)]

        x_sb = sb("x_sb", [P, LAG + T, KD, B])
        wx_sb = sb("wx_sb", [P, KD, 4 * H])
        wh_sb = sb("wh_sb", [P, M, 4 * H])
        w_hi = sb("w_hi", [P, M, 4 * H], F16)
        w_lo = sb("w_lo", [P, M, 4 * H], F16)
        w_scaled = sb("w_scaled", [P, M, 4 * H])
        bias_sb = sb("bias_sb", [P, C])
        w_max = sb("w_max", [P, 1])
        w_top = sb("w_top", [P, 1])
        scale_w = sb("scale_w", [P, 1])
        scale_a = sb("scale_a", [P, 1])
        unscale = sb("unscale", [P, 1])
        xw_sb = sb("xw_sb", [P, R, C, U, X_PARTS, B], BF16)
        xw_whole = sb("xw_whole", [P, C, U, B])
        xw_left = sb("xw_left", [P, C, U, B])
        ident = sb("ident", [P, P], BF16)
        h0_sb = sb("h0_sb", [P, M, B])
        h_parts = sb("h_parts", [P, 2, M, 2, B], F16)
        h_ring = sb("h_ring", [P, U, M, B])
        acts = sb("acts", [P, 2, M, 5, B])
        o_gate = sb("o_gate", [P, 2, M, B])
        prods = sb("prods", [P, 2, M, 2, B])
        out_sb = sb("out_sb", [P, LAG + T, M, B])

        gate_ps = [[bank(f"gate_ps{p}{m}") for m in range(M)] for p in range(2)]
        chain_ps = [bank(f"chain_ps{m}") for m in range(M)]
        xw_ps = bank("xw_ps")
        sums = [chain_ps[m][:, 0:4 * B] for m in range(M)]
        cell = [chain_ps[m][:, 16:16 + B] for m in range(M)]
        tanh_c = [chain_ps[m][:, 32:32 + B] for m in range(M)]

        x_in = sem("x_in")
        x_rest_in = sem("x_rest_in")
        wx_in = sem("wx_in")
        bias_in = sem("bias_in")
        wh_in = sem("wh_in")
        h0_in = sem("h0_in")
        ident_made = sem("ident_made")
        w_max_done = sem("w_max_done")
        w_top_done = sem("w_top_done")
        scales_done = sem("scales_done")
        wx_halved = sem("wx_halved")
        bias_scaled = sem("bias_scaled")
        wh_halved = sem("wh_halved")
        w_hi_done = sem("w_hi_done")
        w_lo_done = sem("w_lo_done")
        h0_scaled = sem("h0_scaled")
        cleared = sem("cleared")
        xw_done = sem("xw_done")
        xw_whole_done = sem("xw_whole_done")
        xw_part0_done = sem("xw_part0_done")
        xw_left_done = sem("xw_left_done")
        xw_part1_done = sem("xw_part1_done")
        xw_cut = sem("xw_cut")
        gates_done = sems("gates_done")
        sums_done = sems("sums_done")
        acts_done = sems("acts_done")
        prods_done = sems("prods_done")
        c_done = sems("c_done")
        tanh_c_done = sems("tanh_c_done")
        h_hi_done = sems("h_hi_done")
        h_done = sems("h_done")
        h_lo_done = sems("h_lo_done")
        out_done = sem("out_done")
        out_stored = sem("out_stored")

        block = ctx.enter_context(nc.Block())


        @block.sync
        def _(sp):
            first = AHEAD * U
            sp.dma_start(wx_sb[:], w_x.rearrange("(k p) n -> p k n", p=P)).then_inc(wx_in, 16)
            sp.dma_start(x_sb[:, LAG:LAG + first], x_p[:, 0:first]).then_inc(x_in, 16)
            sp.dma_start(wh_sb[:], w_h.rearrange("(k p) n -> p k n", p=P)).then_inc(wh_in, 16)
            sp.dma_start(bias_sb[:], bias).then_inc(bias_in, 16)
            sp.dma_start(h0_sb[:], h0_p).then_inc(h0_in, 16)
            sp.dma_start(x_sb[:, LAG + first:], x_p[:, first:]).then_inc(x_rest_in, 16)
            stored = 0
            for n, groups in enumerate(STORES):
                sp.wait_ge(out_done, groups)
                until = min(groups * U - LAG, T)
                sp.dma_start(out_p[:, stored:until], out_sb[:, LAG + stored:LAG + until])\
                  .then_inc(out_stored, 16)
                stored = until
            sp.wait_ge(out_stored, 16 * len(STORES))

        @block.gpsimd
        def _(pool):
            pool.memset(ident[:], 0.0).then_inc(ident_made, 1)
            pool.wait_ge(ident_made, 1)
            pool.affine_select(out=ident[:], in_=ident[:], compare_op=ALU.not_equal, fill=1.0, base=0,
                               pattern=[[-1, P]], channel_multiplier=1).then_inc(ident_made, 1)
            pool.wait_ge(w_max_done, 1)
            pool.partition_all_reduce(w_top[:], w_max[:], P, RMAX).then_inc(w_top_done, 1)
            pool.wait_ge(w_hi_done, 2)
            pool.tensor_tensor(w_lo[:], w_scaled[:], w_hi[:], ALU.subtract).then_inc(w_lo_done, 1)

        def w_tile(w, m, g, k):
            at = GATES[g] * H + m * P
            return w[:, k, at:at + P]

        def step_ps(p, m):
            return gate_ps[p][m][:, 0:4 * 2 * B].rearrange("p (g s b) -> p g s b", g=4, s=2)

        @block.tensor
        def _(pe):
            def put_inputs(p, m, r, u, start):
                parts = xw_sb[:, r, 4 * m:4 * m + 4, u]
                pe.matmul(step_ps(p, m), ident[:], parts[:, :, 0:2], start=start, stop=False,
                          skip_group_check=True)
                return pe.matmul(step_ps(p, m)[:, :, 0], ident[:], parts[:, :, 2], start=False,
                                 stop=not start, skip_group_check=True)

            def low_weights(p, k, m, gates=range(4)):
                h = h_parts[:, 1 - p, k, 0, :]
                for g in gates:
                    pe.matmul(step_ps(p, m)[:, g, 0, :], w_tile(w_lo, m, g, k), h,
                              start=False, stop=False, skip_group_check=True)

            def high_weights(p, k, m, gates=range(4)):
                h = h_parts[:, 1 - p, k]
                for g in gates:
                    mm = pe.matmul(step_ps(p, m)[:, g, 0:2], w_tile(w_hi, m, g, k), h,
                                   start=False, stop=(k == M - 1), skip_group_check=True)
                return mm

            def input_product(chunk, k, ts, n):
                m, g = divmod(chunk, 4)
                return pe.matmul(xw_ps[:, chunk * n * B:(chunk + 1) * n * B], w_tile(wx_sb, m, g, k),
                                 x_sb[:, ts, k, :], start=(k == 0), stop=(k == KD - 1))

            def step(r, u, inputs):
                p = (u + 1) % 2
                if u == U - 1:
                    pe.wait_ge(xw_cut, r + 2)
                for m in range(M):
                    put_inputs(p, m, r + (u + 1) // U, (u + 1) % U, True)
                if inputs:
                    if u == 0:
                        pe.wait_ge(xw_whole_done, r + AHEAD)
                    for i in range(C * KD):
                        if 1 + i * (U - 2) // (C * KD) == u:
                            mm = input_product(i // KD, i % KD, bass.ds((r + AHEAD) * U + LAG, U), U)
                            if i == C * KD - 1:
                                mm.then_inc(xw_done, 1)
                pe.wait_ge(h_hi_done[0], r * U + u + 1)
                low_weights(p, 0, 0)
                low_weights(p, 0, 1)
                pe.wait_ge(h_hi_done[1], r * U + u + 1)
                low_weights(p, 1, 0)
                low_weights(p, 1, 1, range(2))
                pe.wait_ge(h_lo_done[0], r * U + u + 1)
                high_weights(p, 0, 0)
                pe.wait_ge(h_lo_done[1], r * U + u + 1)
                high_weights(p, 1, 0).then_inc(gates_done[0], 1)
                high_weights(p, 0, 1)
                low_weights(p, 1, 1, range(2, 4))
                high_weights(p, 1, 1).then_inc(gates_done[1], 1)

            pe.wait_ge(wx_halved, 1)
            pe.wait_ge(x_in, 16)
            for chunk in range(C):
                for k in range(KD):
                    mm = input_product(chunk, k, slice(LAG, LAG + AHEAD * U), AHEAD * U)
            mm.then_inc(xw_done, 1)
            pe.wait_ge(h0_scaled, 1)
            pe.wait_ge(wh_halved, 1)
            for m in range(M):
                for g in range(4):
                    for k in range(M):
                        pe.matmul(step_ps(0, m)[:, g, 0, :], w_tile(wh_sb, m, g, k), h0_sb[:, k, :],
                                  start=(g == 0 and k == 0), stop=False, skip_group_check=True)
                if m == 0:
                    pe.wait_ge(ident_made, 2)
                    pe.wait_ge(xw_cut, 1)
                put_inputs(0, m, 0, 0, False).then_inc(gates_done[m], 1)
            pe.wait_ge(w_lo_done, 1)
            pe.wait_ge(x_rest_in, 16)
            with pe.Fori(0, R - AHEAD) as r:
                for u in range(U):
                    step(r, u, True)
            for t in range((R - AHEAD) * U, T - 1):
                step(t // U, t % U, False)

        @block.scalar
        def _(act):
            act.preload_act_table(ACT.Tanh)
            act.wait_ge(wh_halved, 1)
            act.wait_ge(scales_done, 2)
            act.activation(w_scaled[:], wh_sb[:], ACT.Copy, scale=scale_w[:, 0:1]).then_inc(w_hi_done, 1)
            act.activation(w_hi[:], wh_sb[:], ACT.Copy, scale=scale_w[:, 0:1]).then_inc(w_hi_done, 1)
            unscale_reg = act.alloc_register("unscale_reg")
            act.load(unscale_reg, unscale[0:1, 0:1].bitcast(I32))

            def gates(p, m, t):
                act.wait_ge(sums_done[m], t + 1)
                act.activation(acts[:, p, m, 0:4, :], sums[m], ACT.Tanh, scale=unscale_reg)\
                   .then_inc(acts_done[m], 1)

            def out_gate(p, m, t):
                act.wait_ge(acts_done[m], t + 1)
                act.activation(o_gate[:, p, m], acts[:, p, m, O], ACT.Copy, scale=2.0 ** (H_BITS - 1),
                               bias=2.0 ** (H_BITS - 1))

            def cell_tanh(p, m, t):
                act.wait_ge(c_done[m], t + 1)
                act.activation(tanh_c[m], cell[m], ACT.Tanh, scale=0.5).then_inc(tanh_c_done[m], 1)

            with act.Fori(0, R) as r:
                for u in range(U):
                    p, t = u % 2, r * U + u
                    gates(p, 0, t)
                    gates(p, 1, t)
                    out_gate(p, 0, t)
                    cell_tanh(p, 0, t)
                    out_gate(p, 1, t)
                    cell_tanh(p, 1, t)

        @block.vector
        def _(dve):
            dve.wait_ge(wx_in, 16)
            dve.tensor_scalar(wx_sb[:, :, 0:3 * H], wx_sb[:, :, 0:3 * H], 0.5, None, ALU.mult)\
               .then_inc(wx_halved, 1)
            dve.wait_ge(wh_in, 16)
            dve.tensor_reduce(w_max[:], wh_sb[:], AX.XY, ALU.max, apply_absolute_value=True)\
               .then_inc(w_max_done, 1)
            dve.memset(x_sb[:, 0:LAG], 0.0).then_inc(cleared, 1)
            dve.memset(h_ring[:, 0:LAG], 0.0).then_inc(cleared, 1)
            dve.memset(acts[:, 0, :, 4, :], 0.0).then_inc(cleared, 1)
            dve.wait_ge(w_max_done, 1)
            dve.tensor_scalar(wh_sb[:, :, 0:3 * H], wh_sb[:, :, 0:3 * H], 0.5, None, ALU.mult)\
               .then_inc(wh_halved, 1)
            dve.wait_ge(w_top_done, 1)
            top_bits = w_top[:].bitcast(I32)
            dve.tensor_scalar(top_bits, top_bits, 0x7F800000, None, ALU.bitwise_and).then_inc(w_top_done, 1)
            dve.wait_ge(w_top_done, 2)
            dve.tensor_scalar(w_top[:], w_top[:], LEAST, None, ALU.max).then_inc(w_top_done, 1)
            dve.wait_ge(w_top_done, 3)
            dve.tensor_scalar(scale_w[:].bitcast(I32), top_bits, -1.0, float((254 + W_TOP) << 23),
                              ALU.mult, ALU.add).then_inc(scales_done, 1)
            dve.tensor_scalar(unscale[:], w_top[:], 2.0 ** -(W_TOP + H_BITS), None, ALU.mult)\
               .then_inc(scales_done, 1)
            dve.wait_ge(scales_done, 2)
            dve.tensor_scalar(scale_a[:], scale_w[:], 2.0 ** H_BITS, None, ALU.mult).then_inc(scales_done, 1)
            dve.wait_ge(scales_done, 3)
            dve.wait_ge(h0_in, 16)
            dve.tensor_scalar(h0_sb[:], h0_sb[:], scale_a[:, 0:1], None, ALU.mult).then_inc(h0_scaled, 1)
            dve.wait_ge(bias_in, 16)
            bias_v = bias_sb[:].rearrange("p (m g) -> p m g", m=M)
            dve.tensor_scalar(bias_v[:, :, 0:3], bias_v[:, :, 0:3], 0.5, scale_a[:, 0:1], ALU.mult, ALU.mult)\
               .then_inc(bias_scaled, 1)
            dve.tensor_scalar(bias_v[:, :, 3:4], bias_v[:, :, 3:4], scale_a[:, 0:1], None, ALU.mult)\
               .then_inc(bias_scaled, 1)
            dve.wait_ge(bias_scaled, 2)

            def input_whole(ps, r):
                dve.scalar_tensor_tensor(out=xw_whole[:].rearrange("p c u b -> p c (u b)"), in0=ps,
                                         scalar=scale_a[:, 0:1],
                                         in1=bias_sb[:].unsqueeze(2).to_broadcast([P, C, UB]),
                                         op0=ALU.mult, op1=ALU.add).then_inc(xw_whole_done, 1)

            whole, left = (a[:].rearrange("p c u b -> p (c u) b") for a in (xw_whole, xw_left))

            def input_part(r, part):
                return xw_sb[:, r].rearrange("p c u s b -> p (c u) s b")[:, :, part]

            def cut_part0(r):
                dve.wait_ge(xw_whole_done, r + 1)
                dve.tensor_copy(input_part(r, 0), whole).then_inc(xw_part0_done, 1)

            def cut_left(r):
                dve.wait_ge(xw_part0_done, r + 1)
                dve.tensor_tensor(left, whole, input_part(r, 0), ALU.subtract).then_inc(xw_left_done, 1)

            def cut_part1(r):
                dve.wait_ge(xw_left_done, r + 1)
                dve.tensor_copy(input_part(r, 1), left).then_inc(xw_part1_done, 1)

            def cut_part2(r):
                dve.wait_ge(xw_part1_done, r + 1)
                dve.tensor_tensor(input_part(r, 2), left, input_part(r, 1), ALU.subtract).then_inc(xw_cut, 1)

            CUTS = [cut_part0, cut_left, cut_part1, cut_part2]
            dve.wait_ge(xw_done, 1)
            first_ps = xw_ps[:, 0:C * AHEAD * UB].rearrange("p (c a n) -> p c a n", c=C, a=AHEAD)
            input_whole(first_ps[:, :, 0], 0)
            for cut in CUTS:
                cut(0)
            dve.wait_ge(xw_cut, 1)
            input_whole(first_ps[:, :, 1], 1)
            dve.wait_ge(cleared, 3)
            dve.wait_ge(x_in, 16)
            dve.wait_ge(x_rest_in, 16)

            def add_parts(p, m, t):
                dve.wait_ge(gates_done[m], t + 1)
                dve.tensor_reduce(sums[m].rearrange("p (g b) -> p g b", b=B),
                                  step_ps(p, m).rearrange("p g s b -> p g b s"), AX.X, ALU.add)\
                   .then_inc(sums_done[m], 1)

            def products(p, m, t):
                dve.wait_ge(acts_done[m], t + 1)
                dve.scalar_tensor_tensor(out=prods[:, p, m], in0=acts[:, p, m, I:F + 1], scalar=1.0,
                                         in1=acts[:, p, m, G:G + 2], op0=ALU.add, op1=ALU.mult)\
                   .then_inc(prods_done[m], 1)

            def new_cell(p, m, t):
                dve.wait_ge(prods_done[m], t + 1)
                dve.scalar_tensor_tensor(out=cell[m], in0=prods[:, p, m, 1], scalar=0.5,
                                         in1=prods[:, p, m, 0], op0=ALU.mult, op1=ALU.add)\
                   .then_inc(c_done[m], 1)

            def keep_cell(p, m):
                dve.scalar_tensor_tensor(out=acts[:, 1 - p, m, 4], in0=prods[:, p, m, 1], scalar=0.5,
                                         in1=prods[:, p, m, 0], op0=ALU.mult, op1=ALU.add)

            def h_high(p, m, t):
                dve.wait_ge(tanh_c_done[m], t + 1)
                dve.tensor_tensor(h_parts[:, p, m, 0], o_gate[:, p, m], tanh_c[m], ALU.mult)\
                   .then_inc(h_hi_done[m], 1)

            def h_whole(u, p, m):
                dve.tensor_tensor(h_ring[:, (u + LAG) % U, m], o_gate[:, p, m], tanh_c[m], ALU.mult)\
                   .then_inc(h_done[m], 1)

            def h_low(u, p, m, t):
                dve.wait_ge(h_done[m], t + 1)
                dve.tensor_tensor(h_parts[:, p, m, 1], h_ring[:, (u + LAG) % U, m],
                                  h_parts[:, p, m, 0], ALU.subtract).then_inc(h_lo_done[m], 1)

            def add_x(at, n):
                out, x = (a[:, bass.ds(at, n)].rearrange("p t m b -> p (t m b)") for a in (out_sb, x_sb))
                dve.scalar_tensor_tensor(out=out, in0=h_ring[:, 0:n].rearrange("p u m b -> p (u m b)"),
                                         scalar=2.0 ** -H_BITS, in1=x, op0=ALU.mult, op1=ALU.add)\
                   .then_inc(out_done, 1)

            def group(r, inputs, cut_next):
                for u in range(U):
                    p, t = u % 2, r * U + u
                    add_parts(p, 0, t)
                    add_parts(p, 1, t)
                    products(p, 0, t)
                    new_cell(p, 0, t)
                    products(p, 1, t)
                    keep_cell(p, 0)
                    new_cell(p, 1, t)
                    h_high(p, 0, t)
                    h_whole(u, p, 0)
                    h_high(p, 1, t)
                    h_whole(u, p, 1)
                    h_low(u, p, 0, t)
                    h_low(u, p, 1, t)
                    keep_cell(p, 1)
                    if u == U - 1 - LAG:
                        add_x(r * U, U)
                    if cut_next and u % 2 and u // 2 < len(CUTS):
                        CUTS[u // 2](r + 1)
                    if inputs and u == U - 2:
                        dve.wait_ge(xw_done, r + 2)
                        input_whole(xw_ps[:, 0:C * UB].rearrange("p (c n) -> p c n", c=C), r + AHEAD)

            with dve.Fori(0, R - AHEAD) as r:
                group(r, True, True)
            for r in range(R - AHEAD, R):
                group(r, False, r + 1 < R)
            add_x(T, LAG)


def kernel(**inputs):
    import numpy as np
    import concourse.bacc as bacc
    from concourse.bass_utils import run_bass_kernel_spmd

    x = np.asarray(inputs["x"])
    B, T, D = x.shape
    arrays = {
        "x_p": np.ascontiguousarray(x.reshape(B, T, -1, P).transpose(3, 1, 2, 0)),
        "h0_p": np.ascontiguousarray(np.asarray(inputs["cond_1024"]).reshape(B, -1, P).transpose(2, 1, 0)),
        "w_x": np.ascontiguousarray(inputs["L0_cond_Wx"]),
        "w_h": np.ascontiguousarray(inputs["L0_cond_Wh"]),
        "bias": np.ascontiguousarray(np.asarray(inputs["L0_cond_b"]).reshape(4, -1, P)[GATES]
                                     .transpose(2, 1, 0).reshape(P, -1)),
    }
    nc = bacc.Bacc("TRN2", target_bir_lowering=False, num_devices=1)
    args = [nc.dram_tensor(n, a.shape, F32, kind="ExternalInput").ap() for n, a in arrays.items()]
    out = nc.dram_tensor("out_p", arrays["x_p"].shape, F32, kind="ExternalOutput").ap()
    lstm_residual(nc, *args, out)
    r = run_bass_kernel_spmd(nc, [arrays], core_ids=[0])
    return np.ascontiguousarray(r.results[0]["out_p"].transpose(3, 1, 2, 0)).reshape(B, T, D)
```
